# Optimizing a Trainium2 kernel written in Bass

```python
import numpy as np
import jax
import jax.numpy as jnp

def _softmax(x, axis=-1):
    return jax.nn.softmax(x, axis=axis)

def _gelu(x):
    return jax.nn.gelu(x, approximate=True)

def _silu(x):
    return jax.nn.silu(x)

def _sigmoid(x):
    return jax.nn.sigmoid(x)

def _layernorm(x, axis=-1, eps=1e-05):
    m = jnp.mean(x, axis=axis, keepdims=True)
    v = jnp.var(x, axis=axis, keepdims=True)
    return (x - m) / jnp.sqrt(v + eps)

def _scatter_add(tgt, idx, src, axis=0):
    return tgt.at[idx].add(src)

def _segment_sum(src, seg, n):
    return jax.ops.segment_sum(src, seg, n)
kernel_name = 'mk_cond_seq_d1_seqx_r2_edeae8'

def setup_inputs(seed: int=0):
    np.random.seed(seed)
    _w = jnp.asarray

    def _rec_inputs():
        import jax
        import jax.numpy as jnp
        _rk = jax.random.key(seed)
        x = -0.000125 + 0.9999 * jax.random.normal(jax.random.fold_in(_rk, 1), (16, 512, 512), jnp.float32)
        _lenS = 512 - jax.random.randint(jax.random.fold_in(_rk, 7), (16,), 0, max(1, 512 // 4) + 1, jnp.int32)
        _lenS2 = 512 - jax.random.randint(jax.random.fold_in(_rk, 8), (16,), 0, max(1, 512 // 4) + 1, jnp.int32)
        cond_256 = 0.0061147 + 1.02565 * jax.random.normal(jax.random.fold_in(_rk, 11), (16, 128), jnp.float32)
        return (x, cond_256)
    x, cond_256 = _rec_inputs()

    def _L0_cond_setup():
        import jax, jax.numpy as jnp
        import numpy as np
        DIM = 512
        BN = 128
        H = 128
        DELTA_SCALE = 0.1
        key = jax.random.key(seed)
        ks = jax.random.split(key, 10)
        B, L = (16, 1024)

        def init(k, shape, fan_in):
            bound = 1.0 / np.sqrt(fan_in)
            return jax.random.uniform(k, shape, jnp.float32, -bound, bound)
        return {'x': jax.random.normal(ks[0], (B, L, DIM), jnp.float32), 'h_lang': jax.random.normal(ks[1], (B, H), jnp.float32), 'Wd': init(ks[2], (BN, DIM), DIM), 'bd': init(ks[3], (BN,), DIM), 'Wu': init(ks[4], (DIM, BN), BN), 'bu': init(ks[5], (DIM,), BN), 'Wdd': init(ks[6], (BN * DIM, H), H), 'bdd': init(ks[7], (BN * DIM,), H), 'Wdu': init(ks[8], (DIM * BN, H), H), 'bdu': init(ks[9], (DIM * BN,), H)}
    _L0_cond_all = _L0_cond_setup()
    _L0_cond_in = {k: v for k, v in _L0_cond_all.items() if k in ('Wd', 'bd', 'Wu', 'bu', 'Wdd', 'bdd', 'Wdu', 'bdu')}
    del _L0_cond_all
    return {'x': x, 'cond_256': cond_256, 'L0_cond_Wd': _L0_cond_in['Wd'], 'L0_cond_bd': _L0_cond_in['bd'], 'L0_cond_Wu': _L0_cond_in['Wu'], 'L0_cond_bu': _L0_cond_in['bu'], 'L0_cond_Wdd': _L0_cond_in['Wdd'], 'L0_cond_bdd': _L0_cond_in['bdd'], 'L0_cond_Wdu': _L0_cond_in['Wdu'], 'L0_cond_bdu': _L0_cond_in['bdu']}

def reference(x, cond_256, L0_cond_Wd, L0_cond_bd, L0_cond_Wu, L0_cond_bu, L0_cond_Wdd, L0_cond_bdd, L0_cond_Wdu, L0_cond_bdu):
    import jax
    import jax.numpy as jnp

    def _L0_cond_ref(x, h_lang, Wd, bd, Wu, bu, Wdd, bdd, Wdu, bdu):
        import jax, jax.numpy as jnp
        import numpy as np
        DIM = 512
        BN = 128
        H = 128
        DELTA_SCALE = 0.1
        B, L, D = x.shape
        dWd = ((h_lang @ Wdd.T + bdd) * DELTA_SCALE).reshape(B, BN, D)
        dWu = ((h_lang @ Wdu.T + bdu) * DELTA_SCALE).reshape(B, D, BN)
        Wd_b = Wd + dWd
        Wu_b = Wu + dWu
        down = jax.nn.relu(jnp.einsum('bld,bnd->bln', x, Wd_b) + bd)
        up = jnp.einsum('bln,bdn->bld', down, Wu_b) + bu
        return x + up
    x = _L0_cond_ref(x, cond_256, L0_cond_Wd, L0_cond_bd, L0_cond_Wu, L0_cond_bu, L0_cond_Wdd, L0_cond_bdd, L0_cond_Wdu, L0_cond_bdu)
    return x

_drawn_inputs = setup_inputs


def setup_inputs(seed=0):
    import zlib

    import numpy as np

    out = dict(_drawn_inputs(seed))
    spreads = {}
    factors = {'L0_cond_bd': 4.969}
    for name, (base, spread) in spreads.items():
        noise = np.random.default_rng([zlib.crc32(name.encode()), seed]).standard_normal(out[name].shape)
        drawn = base * np.exp(spread * noise) if base else spread * noise
        out[name] = jnp.asarray(drawn.astype(out[name].dtype))
    for name, factor in factors.items():
        out[name] = (out[name] * factor).astype(out[name].dtype)
    return out
```

```python
from contextlib import ExitStack

import concourse.bass as bass
from concourse import mybir

BATCH, SEQ, DIM, NECK, COND = 16, 512, 512, 128, 128
P = 128
DCH = DIM // P
QUAD = 32
NQ = P // QUAD
BANK = 512
PER = BANK // QUAD
TILE = NQ * BANK
TILES = NECK * DIM // TILE
CH_TILES = TILES // DCH
RING = 4
GEN_BANKS = 2
MAIN_BANKS = 4
XSEMS = 8
PAIR = BATCH // CH_TILES
DELTA_SCALE = 0.1


def build(nc, wdd, wdu, bases, small, x, out):
    f32 = mybir.dt.float32
    ALU = mybir.AluOpType
    ACT = mybir.ActivationFunctionType

    with ExitStack() as ctx:
        def sbuf(name, shape):
            return ctx.enter_context(nc.sbuf_tensor(name, shape, f32))

        def sem(name):
            return ctx.enter_context(nc.semaphore(name))

        x_sb = sbuf("x_sb", [P, BATCH, DCH, SEQ])
        neck = sbuf("neck", [P, BATCH, DCH * NECK])
        wu = sbuf("wu", [P, 2, BATCH, P])
        ring = sbuf("ring", [P, RING, TILE])
        turned = sbuf("turned", [P, 2, BANK])
        base = sbuf("base", [P, DIM])
        small_sb = sbuf("small_sb", [P, QUAD + 1 + DCH])
        cond_t = small_sb[:, 0:QUAD]
        bd_col = small_sb[:, QUAD:QUAD + 1]
        BU = QUAD + 1
        raw = wu[:, 1].rearrange("p b n -> p (b n)").rearrange("p (k n) -> p k n", k=4)

        gen_ps = [ctx.enter_context(nc.psum_tensor(f"gen_ps{n}", [P, BANK], f32)) for n in range(GEN_BANKS)]
        main_ps = [ctx.enter_context(nc.psum_tensor(f"main_ps{n}", [P, SEQ], f32)) for n in range(MAIN_BANKS)]

        bases_loaded = sem("bases_loaded")
        small_loaded = sem("small_loaded")
        tile_loaded = [sem(f"tile_loaded{n}") for n in range(RING)]
        x_loaded = [sem(f"x_loaded{n}") for n in range(XSEMS)]
        base_made = sem("base_made")
        generated = sem("generated")
        gen_turned = sem("gen_turned")
        weights_ready = sem("weights_ready")
        down_done = sem("down_done")
        relu_done = sem("relu_done")
        up_done = sem("up_done")
        out_ready = sem("out_ready")
        out_stored = sem("out_stored")

        block = ctx.enter_context(nc.Block())

        @block.sync
        def _(sp):
            for s in range(RING):
                sp.dma_start(ring[:, s, :], wdd[s]).then_inc(tile_loaded[s], 16)
            with sp.Fori(1, TILES // RING) as i:
                for s in range(RING):
                    sp.wait_ge(generated, (i - 1) * RING + (s + 1))
                    sp.dma_start(ring[:, s, :], wdd[i * RING + s]).then_inc(tile_loaded[s], 16)
            for k in range(CH_TILES):
                for r in range(PAIR):
                    b = PAIR * k + r
                    if b >= XSEMS:
                        sp.wait_ge(x_loaded[b % XSEMS], 16 * (b // XSEMS))
                    sp.dma_start(x_sb[:, b].rearrange("p c l -> p (c l)"), x[b]).then_inc(x_loaded[b % XSEMS], 16)
                sp.wait_ge(generated, TILES + k - RING + 1)
                sp.dma_start(ring[:, k % RING, :], wdu[k]).then_inc(tile_loaded[k % RING], 16)
            with sp.Fori(CH_TILES // RING, TILES // RING) as i:
                for s in range(RING):
                    sp.wait_ge(generated, i * RING + (TILES - RING + s + 1))
                    sp.dma_start(ring[:, s, :], wdu[i * RING + s]).then_inc(tile_loaded[s], 16)

        @block.tensor
        def _(pe):
            def generate(g, slot, bank, loads, refill):
                pe.wait_ge(tile_loaded[slot], loads * 16)
                if refill:
                    pe.wait_ge(gen_turned, g + (1 - GEN_BANKS))
                for j in range(NQ):
                    last = nc.tensor.matmul(gen_ps[bank][QUAD * j:QUAD * j + QUAD, :], cond_t,
                                            ring[:, slot, j * BANK:(j + 1) * BANK], start=True, stop=True)
                last.then_inc(generated, 1)

            pe.wait_ge(small_loaded, 16)
            for g in range(RING):
                generate(g, g, g % GEN_BANKS, 1, g >= GEN_BANKS)
            with pe.Fori(1, TILES // RING) as i:
                for s in range(RING):
                    generate(i * RING + s, s, s % GEN_BANKS, i + 1, True)

            pe.wait_ge(weights_ready, TILES)
            for k in range(CH_TILES):
                for b in range(PAIR * k, PAIR * k + PAIR):
                    pe.wait_ge(x_loaded[b % XSEMS], 16 * (b // XSEMS + 1))
                    if b >= MAIN_BANKS:
                        pe.wait_ge(relu_done, b - MAIN_BANKS + 1)
                    for c in range(DCH):
                        last = nc.tensor.matmul(main_ps[b % MAIN_BANKS][:, :],
                                                neck[:, b, c * NECK:(c + 1) * NECK], x_sb[:, b, c, :],
                                                start=(c == 0), stop=(c == DCH - 1))
                    last.then_inc(down_done, 1)
                g = TILES + k
                generate(g, g % RING, g % GEN_BANKS, g // RING + 1, True)

            pe.wait_ge(relu_done, BATCH)
            for c in range(DCH):
                pe.wait_ge(weights_ready, TILES + (c + 1) * CH_TILES)
                for k in range(CH_TILES):
                    if c < DCH - 1:
                        g = TILES + (c + 1) * CH_TILES + k
                        generate(g, g % RING, g % GEN_BANKS, g // RING + 1, True)
                    for b in range(PAIR * k, PAIR * k + PAIR):
                        u = c * BATCH + b
                        if u >= MAIN_BANKS:
                            pe.wait_ge(out_ready, u - MAIN_BANKS + 1)
                        nc.tensor.matmul(main_ps[u % MAIN_BANKS][:, :], wu[:, c % 2, b, :],
                                         neck[:, b, :], start=True, stop=True).then_inc(up_done, 1)

        @block.vector
        def _(dve):
            def make_base(which):
                nc.vector.scalar_tensor_tensor(out=base[:, :], in0=raw[:, 2 * which + 1, :], scalar=DELTA_SCALE,
                                               in1=raw[:, 2 * which, :], op0=ALU.mult, op1=ALU.add)\
                    .then_inc(base_made, 1)
                dve.wait_ge(base_made, which + 1)

            def turn(g, bank):
                dve.wait_ge(generated, g + 1)
                nc.vector.transpose(turned[:, bank, :], gen_ps[bank][:, :]).then_inc(gen_turned, 1)
                dve.wait_ge(gen_turned, g + 1)

            def place(dst, bank, base_cols):
                delta = turned[:, bank, :].rearrange("p (q b) -> p b q", b=QUAD)[:, 0:BATCH, :]
                nc.vector.scalar_tensor_tensor(out=dst, in0=delta, scalar=DELTA_SCALE,
                                               in1=base_cols.unsqueeze(1).to_broadcast([P, BATCH, PER]),
                                               op0=ALU.mult, op1=ALU.add).then_inc(weights_ready, 1)

            dve.wait_ge(bases_loaded, 16)
            make_base(0)
            with dve.Fori(0, TILES // GEN_BANKS) as i:
                for s in range(GEN_BANKS):
                    turn(i * GEN_BANKS + s, s)
                    col = i * (GEN_BANKS * PER) + s * PER
                    place(neck[:, :, bass.ds(col, PER)], s, base[:, bass.ds(col, PER)])
            dve.wait_ge(weights_ready, TILES)
            make_base(1)
            with dve.Fori(0, CH_TILES // GEN_BANKS) as i:
                for s in range(GEN_BANKS):
                    turn(i * GEN_BANKS + (TILES + s), s)
                    col = i * (GEN_BANKS * PER) + s * PER
                    place(wu[:, 0, :, bass.ds(col, PER)], s, base[:, bass.ds(col, PER)])
            for c in range(DCH):
                with dve.Fori(0, CH_TILES // GEN_BANKS) as i:
                    for s in range(GEN_BANKS):
                        if c < DCH - 1:
                            turn(i * GEN_BANKS + (TILES + (c + 1) * CH_TILES + s), s)
                            col = i * (GEN_BANKS * PER) + s * PER
                            place(wu[:, (c + 1) % 2, :, bass.ds(col, PER)], s,
                                  base[:, bass.ds(col + (c + 1) * P, PER)])
                        for r in range(PAIR):
                            n = s * PAIR + r
                            dve.wait_ge(up_done, i * MAIN_BANKS + (c * BATCH + n + 1))
                            xo = x_sb[:, bass.ds(i * MAIN_BANKS + n, 1), c, :].rearrange("p b l -> p (b l)")
                            nc.vector.scalar_tensor_tensor(out=xo, in0=main_ps[n][:, :],
                                                           scalar=small_sb[:, BU + c:BU + c + 1], in1=xo,
                                                           op0=ALU.add, op1=ALU.add).then_inc(out_ready, 1)

        @block.scalar
        def _(act):
            act.dma_start(small_sb[:, :], small).then_inc(small_loaded, 16)
            act.dma_start(wu[:, 1].rearrange("p b n -> p (b n)"), bases).then_inc(bases_loaded, 16)
            act.wait_ge(small_loaded, 16)
            with act.Fori(0, BATCH // MAIN_BANKS) as i:
                for s in range(MAIN_BANKS):
                    act.wait_ge(down_done, i * MAIN_BANKS + (s + 1))
                    dst = neck[:, bass.ds(i * MAIN_BANKS + s, 1), :].rearrange("p b n -> p (b n)")
                    nc.scalar.activation(dst, main_ps[s][:, :], ACT.Relu, bias=bd_col).then_inc(relu_done, 1)
            for c in range(DCH):
                for k in range(BATCH // PAIR):
                    act.wait_ge(out_ready, c * BATCH + (k + 1) * PAIR)
                    act.dma_start(out[c, k].rearrange("p (b l) -> p b l", b=PAIR),
                                  x_sb[:, k * PAIR:(k + 1) * PAIR, c, :]).then_inc(out_stored, 16)
            act.wait_ge(out_stored, 16 * DCH * BATCH // PAIR)


def kernel(x, cond_256, L0_cond_Wd, L0_cond_bd, L0_cond_Wu, L0_cond_bu, L0_cond_Wdd, L0_cond_bdd,
           L0_cond_Wdu, L0_cond_bdu):
    import numpy as np
    import concourse.bacc as bacc
    from concourse.bass_utils import run_bass_kernel_spmd

    def lay(a):
        return np.ascontiguousarray(a)

    Wd, bd, Wu, bu, Wdd, bdd, Wdu, bdu = (np.asarray(a) for a in (
        L0_cond_Wd, L0_cond_bd, L0_cond_Wu, L0_cond_bu, L0_cond_Wdd, L0_cond_bdd, L0_cond_Wdu, L0_cond_bdu))
    wdd = Wdd.reshape(CH_TILES, PER, DCH, NQ, QUAD, COND).transpose(2, 0, 5, 3, 1, 4)
    wdu = Wdu.reshape(TILES, PER, NQ, QUAD, COND).transpose(0, 4, 2, 1, 3)
    bases = [a.reshape(NECK, DCH, P).transpose(2, 1, 0).reshape(P, DIM) for a in (Wd, bdd)]
    bases += [a.reshape(DIM, NECK).T for a in (Wu, bdu)]
    pad = np.zeros((COND, QUAD - BATCH), np.float32)
    arrays = {
        "wdd": lay(wdd.reshape(TILES, COND, TILE)),
        "wdu": lay(wdu.reshape(TILES, COND, TILE)),
        "bases": lay(np.concatenate([bases[0], bases[1], bases[2], bases[3]], axis=1)),
        "small": lay(np.concatenate([np.asarray(cond_256).T, pad, bd[:, None], bu.reshape(DCH, P).T], axis=1)),
        "x": lay(np.asarray(x).transpose(0, 2, 1).reshape(BATCH, DCH, P, SEQ).transpose(0, 2, 1, 3)
                 .reshape(BATCH, P, DCH * SEQ)),
    }
    nc = bacc.Bacc("TRN2", target_bir_lowering=False, num_devices=1, dynamic_dma_scratch_size=8192)
    args = [nc.dram_tensor(n, a.shape, mybir.dt.from_np(a.dtype), kind="ExternalInput").ap()
            for n, a in arrays.items()]
    out = nc.dram_tensor("out", (DCH, BATCH // PAIR, P, PAIR * SEQ), mybir.dt.float32, kind="ExternalOutput").ap()
    build(nc, *args, out)
    got = run_bass_kernel_spmd(nc, [arrays], core_ids=[0]).results[0]["out"]
    got = got.reshape(DCH, BATCH // PAIR, P, PAIR, SEQ).transpose(1, 3, 4, 0, 2)
    return lay(got.reshape(BATCH, SEQ, DIM))
```

```python
from contextlib import ExitStack

import concourse.bass as bass
from concourse import mybir

BATCH, SEQ, DIM, NECK, COND = 16, 512, 512, 128, 128
P = 128
DCH = DIM // P
QUAD = 32
NQ = P // QUAD
BANK = 512
PER = BANK // QUAD
TILE = NQ * BANK
TILES = NECK * DIM // TILE
CH_TILES = TILES // DCH
RING = 4
GEN_BANKS = 2
MAIN_BANKS = 4
PAIR = BATCH // CH_TILES
GROUP = 2 * PAIR
HELD = 2 * GROUP
DELTA_SCALE = 0.1
assert PAIR * GEN_BANKS == MAIN_BANKS


def build(nc, wdd, wdu, bases, small, x, out):
    f32 = mybir.dt.float32
    ALU = mybir.AluOpType
    ACT = mybir.ActivationFunctionType

    with ExitStack() as ctx:
        def sbuf(name, shape):
            return ctx.enter_context(nc.sbuf_tensor(name, shape, f32))

        def sem(name):
            return ctx.enter_context(nc.semaphore(name))

        x_sb = sbuf("x_sb", [P, DCH, BATCH, SEQ])
        neck = sbuf("neck", [P, BATCH, DCH * NECK])
        wu = sbuf("wu", [P, 2, BATCH, P])
        ring = sbuf("ring", [P, RING, TILE])
        turned = sbuf("turned", [P, 2, BANK])
        base = sbuf("base", [P, DIM])
        small_sb = sbuf("small_sb", [P, QUAD + 1 + DCH])
        cond_t = small_sb[:, 0:QUAD]
        bd_col = small_sb[:, QUAD:QUAD + 1]
        BU = QUAD + 1
        raw = wu[:, 1].rearrange("p b n -> p (b n)").rearrange("p (k n) -> p k n", k=4)

        gen_ps = [ctx.enter_context(nc.psum_tensor(f"gen_ps{n}", [P, BANK], f32)) for n in range(GEN_BANKS)]
        main_ps = [ctx.enter_context(nc.psum_tensor(f"main_ps{n}", [P, SEQ], f32)) for n in range(MAIN_BANKS)]

        bases_loaded = sem("bases_loaded")
        small_loaded = sem("small_loaded")
        tile_loaded = [sem(f"tile_loaded{n}") for n in range(RING)]
        x_loaded = [sem(f"x_loaded{n}") for n in range(BATCH // PAIR)]
        base_made = sem("base_made")
        generated = sem("generated")
        gen_turned = sem("gen_turned")
        weights_ready = sem("weights_ready")
        down_done = sem("down_done")
        relu_done = sem("relu_done")
        up_done = sem("up_done")
        out_ready = sem("out_ready")
        out_stored = sem("out_stored")

        block = ctx.enter_context(nc.Block())

        @block.sync
        def _(sp):
            def load_x(k):
                sp.dma_start(x_sb[:, :, k * PAIR:(k + 1) * PAIR, :].rearrange("p c b l -> p c (b l)"),
                             x[k]).then_inc(x_loaded[k], 16)

            for s in range(RING):
                sp.dma_start(ring[:, s, :], wdd[s]).then_inc(tile_loaded[s], 16)
            with sp.Fori(1, TILES // RING - 1) as i:
                for s in range(RING):
                    sp.wait_ge(generated, (i - 1) * RING + (s + 1))
                    sp.dma_start(ring[:, s, :], wdd[i * RING + s]).then_inc(tile_loaded[s], 16)
            load_x(0)
            for t in range(TILES - RING, TILES):
                sp.wait_ge(generated, t - RING + 1)
                sp.dma_start(ring[:, t % RING, :], wdd[t]).then_inc(tile_loaded[t % RING], 16)
            for k in range(CH_TILES):
                if k + 1 < BATCH // PAIR:
                    load_x(k + 1)
                sp.wait_ge(generated, TILES + k - RING + 1)
                sp.dma_start(ring[:, k % RING, :], wdu[k]).then_inc(tile_loaded[k % RING], 16)
            with sp.Fori(CH_TILES // RING, TILES // RING) as i:
                for s in range(RING):
                    sp.wait_ge(generated, i * RING + (TILES - RING + s + 1))
                    sp.dma_start(ring[:, s, :], wdu[i * RING + s]).then_inc(tile_loaded[s], 16)

        @block.tensor
        def _(pe):
            def generate(g, slot, bank, loads, refill):
                pe.wait_ge(tile_loaded[slot], loads * 16)
                if refill:
                    pe.wait_ge(gen_turned, g + (1 - GEN_BANKS))
                for j in range(NQ):
                    last = nc.tensor.matmul(gen_ps[bank][QUAD * j:QUAD * j + QUAD, :], cond_t,
                                            ring[:, slot, j * BANK:(j + 1) * BANK], start=True, stop=True)
                last.then_inc(generated, 1)

            pe.wait_ge(small_loaded, 16)
            for g in range(RING):
                generate(g, g, g % GEN_BANKS, 1, g >= GEN_BANKS)
            with pe.Fori(1, TILES // RING) as i:
                for s in range(RING):
                    generate(i * RING + s, s, s % GEN_BANKS, i + 1, True)

            pe.wait_ge(weights_ready, TILES)
            for k in range(CH_TILES):
                pe.wait_ge(x_loaded[k], 16)
                for b in range(PAIR * k, PAIR * k + PAIR):
                    if b >= MAIN_BANKS:
                        pe.wait_ge(relu_done, b - MAIN_BANKS + 1)
                    for c in range(DCH):
                        last = nc.tensor.matmul(main_ps[b % MAIN_BANKS][:, :],
                                                neck[:, b, c * NECK:(c + 1) * NECK], x_sb[:, c, b, :],
                                                start=(c == 0), stop=(c == DCH - 1))
                    last.then_inc(down_done, 1)
                g = TILES + k
                generate(g, g % RING, g % GEN_BANKS, g // RING + 1, True)

            pe.wait_ge(relu_done, BATCH)
            for c in range(DCH):
                pe.wait_ge(weights_ready, TILES + (c + 1) * CH_TILES)
                for k in range(CH_TILES):
                    if c < DCH - 1:
                        g = TILES + (c + 1) * CH_TILES + k
                        generate(g, g % RING, g % GEN_BANKS, g // RING + 1, True)
                    for b in range(PAIR * k, PAIR * k + PAIR):
                        u = c * BATCH + b
                        if u >= MAIN_BANKS:
                            pe.wait_ge(out_ready, u - MAIN_BANKS + 1)
                        nc.tensor.matmul(main_ps[u % MAIN_BANKS][:, :], wu[:, c % 2, b, :],
                                         neck[:, b, :], start=True, stop=True).then_inc(up_done, 1)

        @block.vector
        def _(dve):
            def make_base(which):
                nc.vector.scalar_tensor_tensor(out=base[:, :], in0=raw[:, 2 * which + 1, :], scalar=DELTA_SCALE,
                                               in1=raw[:, 2 * which, :], op0=ALU.mult, op1=ALU.add)\
                    .then_inc(base_made, 1)
                dve.wait_ge(base_made, which + 1)

            def turn(g, bank):
                dve.wait_ge(generated, g + 1)
                nc.vector.transpose(turned[:, bank, :], gen_ps[bank][:, :]).then_inc(gen_turned, 1)
                dve.wait_ge(gen_turned, g + 1)

            def place(dst, bank, base_cols):
                delta = turned[:, bank, :].rearrange("p (q b) -> p b q", b=QUAD)[:, 0:BATCH, :]
                nc.vector.scalar_tensor_tensor(out=dst, in0=delta, scalar=DELTA_SCALE,
                                               in1=base_cols.unsqueeze(1).to_broadcast([P, BATCH, PER]),
                                               op0=ALU.mult, op1=ALU.add).then_inc(weights_ready, 1)

            dve.wait_ge(bases_loaded, 16)
            make_base(0)
            with dve.Fori(0, TILES // GEN_BANKS) as i:
                for s in range(GEN_BANKS):
                    turn(i * GEN_BANKS + s, s)
                    col = i * (GEN_BANKS * PER) + s * PER
                    place(neck[:, :, bass.ds(col, PER)], s, base[:, bass.ds(col, PER)])
            dve.wait_ge(weights_ready, TILES)
            make_base(1)
            with dve.Fori(0, CH_TILES // GEN_BANKS) as i:
                for s in range(GEN_BANKS):
                    turn(i * GEN_BANKS + (TILES + s), s)
                    col = i * (GEN_BANKS * PER) + s * PER
                    place(wu[:, 0, :, bass.ds(col, PER)], s, base[:, bass.ds(col, PER)])
            for c in range(DCH):
                with dve.Fori(0, CH_TILES // GEN_BANKS) as i:
                    for s in range(GEN_BANKS):
                        if c < DCH - 1:
                            turn(i * GEN_BANKS + (TILES + (c + 1) * CH_TILES + s), s)
                            col = i * (GEN_BANKS * PER) + s * PER
                            place(wu[:, (c + 1) % 2, :, bass.ds(col, PER)], s,
                                  base[:, bass.ds(col + (c + 1) * P, PER)])
                        for r in range(PAIR):
                            n = s * PAIR + r
                            dve.wait_ge(up_done, i * MAIN_BANKS + (c * BATCH + n + 1))
                            xo = x_sb[:, c, bass.ds(i * MAIN_BANKS + n, 1), :].rearrange("p b l -> p (b l)")
                            nc.vector.scalar_tensor_tensor(out=xo, in0=main_ps[n][:, :],
                                                           scalar=small_sb[:, BU + c:BU + c + 1], in1=xo,
                                                           op0=ALU.add, op1=ALU.add).then_inc(out_ready, 1)

        @block.scalar
        def _(act):
            act.dma_start(small_sb[:, :], small).then_inc(small_loaded, 16)
            act.dma_start(wu[:, 1].rearrange("p b n -> p (b n)"), bases).then_inc(bases_loaded, 16)
            act.wait_ge(small_loaded, 16)
            with act.Fori(0, BATCH // MAIN_BANKS) as i:
                for s in range(MAIN_BANKS):
                    act.wait_ge(down_done, i * MAIN_BANKS + (s + 1))
                    dst = neck[:, bass.ds(i * MAIN_BANKS + s, 1), :].rearrange("p b n -> p (b n)")
                    nc.scalar.activation(dst, main_ps[s][:, :], ACT.Relu, bias=bd_col).then_inc(relu_done, 1)
            def store(c, b, n):
                act.wait_ge(out_ready, c * BATCH + b + n)
                act.dma_start(out[c, b // GROUP, :, b % GROUP:b % GROUP + n, :],
                              x_sb[:, c, b:b + n, :]).then_inc(out_stored, 16)

            for c in range(DCH - 1):
                for b in range(0, BATCH, GROUP):
                    if c == DCH - 2 and b == BATCH - HELD:
                        act.wait_ge(tile_loaded[RING - 1], 16 * (2 * TILES // RING))
                    store(c, b, GROUP)
            for b in range(0, BATCH - PAIR, PAIR):
                store(DCH - 1, b, PAIR)
            for b in range(BATCH - PAIR, BATCH):
                store(DCH - 1, b, 1)
            act.wait_ge(out_stored, 16 * ((DCH - 1) * BATCH // GROUP + BATCH // PAIR + 1))


def kernel(x, cond_256, L0_cond_Wd, L0_cond_bd, L0_cond_Wu, L0_cond_bu, L0_cond_Wdd, L0_cond_bdd,
           L0_cond_Wdu, L0_cond_bdu):
    import numpy as np
    import concourse.bacc as bacc
    from concourse.bass_utils import run_bass_kernel_spmd

    def lay(a):
        return np.ascontiguousarray(a)

    Wd, bd, Wu, bu, Wdd, bdd, Wdu, bdu = (np.asarray(a) for a in (
        L0_cond_Wd, L0_cond_bd, L0_cond_Wu, L0_cond_bu, L0_cond_Wdd, L0_cond_bdd, L0_cond_Wdu, L0_cond_bdu))
    wdd = Wdd.reshape(CH_TILES, PER, DCH, NQ, QUAD, COND).transpose(2, 0, 5, 3, 1, 4)
    wdu = Wdu.reshape(TILES, PER, NQ, QUAD, COND).transpose(0, 4, 2, 1, 3)
    bases = [a.reshape(NECK, DCH, P).transpose(2, 1, 0).reshape(P, DIM) for a in (Wd, bdd)]
    bases += [a.reshape(DIM, NECK).T for a in (Wu, bdu)]
    pad = np.zeros((COND, QUAD - BATCH), np.float32)
    arrays = {
        "wdd": lay(wdd.reshape(TILES, COND, TILE)),
        "wdu": lay(wdu.reshape(TILES, COND, TILE)),
        "bases": lay(np.concatenate([bases[0], bases[1], bases[2], bases[3]], axis=1)),
        "small": lay(np.concatenate([np.asarray(cond_256).T, pad, bd[:, None], bu.reshape(DCH, P).T], axis=1)),
        "x": lay(np.asarray(x).transpose(0, 2, 1).reshape(BATCH // PAIR, PAIR, DCH, P, SEQ)
                 .transpose(0, 3, 2, 1, 4).reshape(BATCH // PAIR, P, DCH, PAIR * SEQ)),
    }
    nc = bacc.Bacc("TRN2", target_bir_lowering=False, num_devices=1, dynamic_dma_scratch_size=8192)
    args = [nc.dram_tensor(n, a.shape, mybir.dt.from_np(a.dtype), kind="ExternalInput").ap()
            for n, a in arrays.items()]
    out = nc.dram_tensor("out", (DCH, BATCH // GROUP, P, GROUP, SEQ), mybir.dt.float32, kind="ExternalOutput").ap()
    build(nc, *args, out)
    got = run_bass_kernel_spmd(nc, [arrays], core_ids=[0]).results[0]["out"]
    got = got.transpose(1, 3, 4, 0, 2)
    return lay(got.reshape(BATCH, SEQ, DIM))
```
